# Optimizing a Trainium2 kernel written in Bass

```python
import numpy as np
import jax
import jax.numpy as jnp

def _softmax(x, axis=-1):
    return jax.nn.softmax(x, axis=axis)
def _gelu(x):
    return jax.nn.gelu(x, approximate=True)
def _silu(x):
    return jax.nn.silu(x)
def _sigmoid(x):
    return jax.nn.sigmoid(x)
def _layernorm(x, axis=-1, eps=1e-5):
    m = jnp.mean(x, axis=axis, keepdims=True)
    v = jnp.var(x, axis=axis, keepdims=True)
    return (x - m) / jnp.sqrt(v + eps)
def _scatter_add(tgt, idx, src, axis=0):
    return tgt.at[idx].add(src)
def _segment_sum(src, seg, n):
    return jax.ops.segment_sum(src, seg, n)

kernel_name = 'mk_conv_seq_d1_conv_nchw16_d1334d'

def setup_inputs(seed: int = 0):
    np.random.seed(seed)
    _w = jnp.asarray
    def _rec_inputs():
        import jax
        import jax.numpy as jnp
        _gk = jax.random.key(seed)
        x = -7.109e-05 + 0.9999 * jax.random.normal(jax.random.fold_in(_gk, 1), (1, 16, 2048, 2048), jnp.float32)
        return x
    x = _rec_inputs()
    def _L0_conv_setup():
        import jax, jax.numpy as jnp
        import numpy as np
        EPS = 1e-06
        key = jax.random.key(seed)
        k0, k1, k2 = jax.random.split(key, 3)
        B, H, S, MW = (1, 16, 2048, 32)
        x = jax.random.normal(k0, (B, H, S, S), dtype=jnp.float32)
        W1 = jax.random.normal(k1, (1, MW), dtype=jnp.float32)
        b1 = jnp.zeros((MW,), dtype=jnp.float32)
        W2 = jax.random.normal(k2, (MW, H), dtype=jnp.float32) * (1.0 / np.sqrt(MW))
        b2 = jnp.zeros((H,), dtype=jnp.float32)
        c = jnp.float32(0.1)
        L_multiplier = jnp.float32(1.0)
        init_L = jnp.float32(512.0)
        return {'x': x, 'W1': W1, 'b1': b1, 'W2': W2, 'b2': b2, 'c': c, 'L_multiplier': L_multiplier, 'init_L': init_L}
    _L0_conv_all = _L0_conv_setup()
    _L0_conv_in = {k: v for k, v in _L0_conv_all.items() if k in ('W1', 'b1', 'W2', 'b2', 'c', 'L_multiplier', 'init_L', )}
    del _L0_conv_all

    return {
        "x": x,
        "L0_conv_W1": _L0_conv_in["W1"],
        "L0_conv_b1": _L0_conv_in["b1"],
        "L0_conv_W2": _L0_conv_in["W2"],
        "L0_conv_b2": _L0_conv_in["b2"],
        "L0_conv_c": _L0_conv_in["c"],
        "L0_conv_L_multiplier": _L0_conv_in["L_multiplier"],
        "L0_conv_init_L": _L0_conv_in["init_L"],
    }

def reference(x, L0_conv_W1, L0_conv_b1, L0_conv_W2, L0_conv_b2, L0_conv_c, L0_conv_L_multiplier, L0_conv_init_L):
    import jax
    import jax.numpy as jnp
    def _L0_conv_ref(x, W1, b1, W2, b2, c, L_multiplier, init_L):
        import jax, jax.numpy as jnp
        import numpy as np
        EPS = 1e-06
        S = x.shape[-1]
        idx = jnp.arange(S)
        rel = jnp.tril(idx[:, None] - idx[None, :]).astype(jnp.float32)
        threshold = jnp.abs(L_multiplier * init_L)
        pos = jnp.maximum(rel.max(axis=-1), threshold)[:, None]
        nd = jnp.log(jnp.abs(c * rel) + 1.0) / (jnp.log(jnp.abs(c * pos) + 1.0) + EPS)
        nd = nd.astype(x.dtype)
        h = jax.nn.relu(nd[..., None] * W1[0] + b1)
        bias = jnp.einsum('qkm,mh->qkh', h, W2) + b2
        return x + bias.transpose(2, 0, 1)[None]

    def _gn(v, G=8, eps=1e-5):
        B_, C_, H_, W_ = v.shape
        g = v.reshape(B_, G, C_ // G, H_, W_)
        m = jnp.mean(g, axis=(2, 3, 4), keepdims=True)
        s = jnp.var(g, axis=(2, 3, 4), keepdims=True)
        return ((g - m) / jnp.sqrt(s + eps)).reshape(v.shape)

    def _ln_c(v, eps=1e-6):
        m = jnp.mean(v, axis=1, keepdims=True)
        s = jnp.var(v, axis=1, keepdims=True)
        return (v - m) / jnp.sqrt(s + eps)

    def _ln_t(v, eps=1e-5):
        m = jnp.mean(v, axis=-1, keepdims=True)
        s = jnp.var(v, axis=-1, keepdims=True)
        return (v - m) / jnp.sqrt(s + eps)

    def _to_tokens(v):
        B_, C_, H_, W_ = v.shape
        return v.reshape(B_, C_, H_ * W_).transpose(0, 2, 1)
    def _from_tokens(t, like):
        B_, C_, H_, W_ = like.shape
        return t.transpose(0, 2, 1).reshape(B_, C_, H_, W_)

    x = _L0_conv_ref(x, L0_conv_W1, L0_conv_b1, L0_conv_W2, L0_conv_b2, L0_conv_c, L0_conv_L_multiplier, L0_conv_init_L)
    return x


_drawn_inputs = setup_inputs


def setup_inputs(seed=0):
    import zlib

    import numpy as np

    out = dict(_drawn_inputs(seed))
    spreads = {'L0_conv_b1': (0.0, 0.1), 'L0_conv_b2': (0.0, 0.1)}
    factors = {}
    for name, (base, spread) in spreads.items():
        noise = np.random.default_rng([zlib.crc32(name.encode()), seed]).standard_normal(out[name].shape)
        drawn = base * np.exp(spread * noise) if base else spread * noise
        out[name] = jnp.asarray(drawn.astype(out[name].dtype))
    for name, factor in factors.items():
        out[name] = (out[name] * factor).astype(out[name].dtype)
    return out
```

```python
from contextlib import ExitStack

import concourse.bass as bass
from concourse import mybir

ALU = mybir.AluOpType
ACT = mybir.ActivationFunctionType
F32 = mybir.dt.float32
P = 128
BANK = 512


def fire_bias_kernel(nc, x, W1, b1, W2, b2, c, L_multiplier, init_L, out):
    EPS = 1e-6
    _, H, S, _ = x.shape
    M = W1.shape[1]
    TILE_ROWS = P // H
    GROUP_ROWS = P // M
    GROUPS = TILE_ROWS // GROUP_ROWS
    BANDS = 8
    BAND_ROWS = S // BANDS
    TURNS = BAND_ROWS // TILE_ROWS
    AHEAD = BANDS // 2
    assert H * TILE_ROWS == P and M * GROUP_ROWS == P and M == 32
    ORDER = [b for n in range(BANDS // 2) for b in (n, BANDS - 1 - n)]
    WIDTH = [(b + 1) * BAND_ROWS for b in ORDER]

    SHIFT = S - GROUP_ROWS
    TABLE = SHIFT + BAND_ROWS

    with ExitStack() as ctx:
        def sb(name, shape):
            return ctx.enter_context(nc.sbuf_tensor(name, shape, F32))

        def sem(name):
            return ctx.enter_context(nc.semaphore(name))

        x_tile = sb("x_tile", [P, BANDS, S])
        hidden = sb("hidden", [P, 2, GROUPS, S])
        log_rel = sb("log_rel", [P, TABLE])
        row_scale = sb("row_scale", [P, S // GROUP_ROWS])
        denominator = sb("denominator", [P, S // GROUP_ROWS])
        threshold = sb("threshold", [P, 1])
        c_col = sb("c_col", [P, 1])
        multiplier_col = sb("multiplier_col", [P, 1])
        init_col = sb("init_col", [P, 1])
        W1_col = sb("W1_col", [P, 1])
        b1_col = sb("b1_col", [P, 1])
        b2_col = sb("b2_col", [P, 1])
        W2_rows = sb("W2_rows", [P, H])
        W2_spread = sb("W2_spread", [P, GROUPS, H, TILE_ROWS])
        hidden_far = sb("hidden_far", [P, 2])
        bias_far = sb("bias_far", [P, 1])
        psum = ctx.enter_context(nc.psum_tensor("bias", [P, 2, S], F32))

        params_loaded = sem("params_loaded")
        W2_loaded = sem("W2_loaded")
        x_loaded = [sem(f"x_loaded{n}") for n in range(BANDS)]
        x_stored = [sem(f"x_stored{n}") for n in range(BANDS)]
        rel_made = sem("rel_made")
        threshold_made = sem("threshold_made")
        cut_made = sem("cut_made")
        abs_made = sem("abs_made")
        log_made = sem("log_made")
        scale_made = sem("scale_made")
        setup_step = sem("setup_step")
        W2_ready = sem("W2_ready")
        hidden_far_ready = sem("hidden_far_ready")
        product_far_ready = sem("product_far_ready")
        bias_far_ready = sem("bias_far_ready")
        hidden_ready = [sem(f"hidden_ready{n}") for n in range(BANDS)]
        product_ready = [sem(f"product_ready{n}") for n in range(BANDS)]
        near_added = [sem(f"near_added{n}") for n in range(BANDS)]
        far_added = [sem(f"far_added{n}") for n in range(BANDS)]

        def rows_of(tensor, n, turn):
            band = tensor[0, :, ORDER[n] * BAND_ROWS:(ORDER[n] + 1) * BAND_ROWS, :]
            return band[:, bass.ds(turn * TILE_ROWS, TILE_ROWS), :]

        def wait_two_back(engine, done, n, turn):
            if n >= 2:
                engine.wait_ge(done[n - 2], turn + 1)
            elif not isinstance(turn, int):
                engine.wait_ge(done[n - 2 + BANDS], turn)

        block = ctx.enter_context(nc.Block())

        @block.sync
        def _(sp):
            def load(n, turn):
                sp.dma_start(x_tile[:, n, :], rows_of(x, n, turn)).then_inc(x_loaded[n], 16)

            def store(n, turn):
                sp.wait_ge(near_added[n], turn + 1)
                if WIDTH[n] < S:
                    sp.wait_ge(far_added[n], turn + 1)
                sp.dma_start(rows_of(out, n, turn), x_tile[:, n, :]).then_inc(x_stored[n], 16)

            def reload(n, turn):
                sp.wait_ge(x_stored[n], turn * 16)
                load(n, turn)

            for scalar, column in ((c, c_col), (L_multiplier, multiplier_col), (init_L, init_col)):
                sp.dma_start(column[:, :], bass.AP(scalar.tensor, 0, [[0, P], [1, 1]])).then_inc(params_loaded, 16)
            for vector, column in ((W1, W1_col), (b1, b1_col)):
                sp.dma_start(column[:, :], bass.AP(vector.tensor, 0, [[0, GROUP_ROWS], [1, M], [1, 1]])).then_inc(params_loaded, 16)
            sp.dma_start(b2_col[:, :], bass.AP(b2.tensor, 0, [[1, H], [0, TILE_ROWS], [1, 1]])).then_inc(params_loaded, 16)
            sp.dma_start(W2_rows[:, :], bass.AP(W2.tensor, 0, [[0, GROUP_ROWS], [H, M], [1, H]])).then_inc(W2_loaded, 16)

            for n in range(BANDS):
                load(n, 0)
            for n in range(BANDS):
                store(n, 0)
                if n >= AHEAD:
                    reload(n - AHEAD, 1)
            with sp.Fori(1, TURNS - 1) as turn:
                for n in range(BANDS):
                    store(n, turn)
                    if n < AHEAD:
                        reload(n + AHEAD, turn)
                    else:
                        reload(n - AHEAD, turn + 1)
            for n in range(BANDS):
                store(n, TURNS - 1)
                if n < AHEAD:
                    reload(n + AHEAD, TURNS - 1)
            for n in range(BANDS):
                sp.wait_ge(x_stored[n], TURNS * 16)

        @block.gpsimd
        def _(pool):
            for r in range(GROUP_ROWS):
                rows = slice(r * M, (r + 1) * M)
                nc.gpsimd.iota(log_rel[rows, :], [[-1, TABLE]], base=SHIFT + r, channel_multiplier=0,
                               allow_small_or_imprecise_dtypes=True).then_inc(rel_made, 1)
                nc.gpsimd.iota(denominator[rows, :], [[GROUP_ROWS, S // GROUP_ROWS]], base=r, channel_multiplier=0,
                               allow_small_or_imprecise_dtypes=True).then_inc(rel_made, 1)

        @block.vector
        def _(dve):
            nc.vector.memset(W2_spread[:], 0.0).then_inc(setup_step, 1)
            dve.wait_ge(setup_step, 1)
            dve.wait_ge(W2_loaded, 16)
            for g in range(GROUPS):
                for r in range(GROUP_ROWS):
                    rows = slice(r * M, (r + 1) * M)
                    nc.vector.tensor_copy(W2_spread[rows, g, :, g * GROUP_ROWS + r], W2_rows[rows, :]).then_inc(W2_ready, 1)
            dve.wait_ge(rel_made, 2 * GROUP_ROWS)
            nc.vector.tensor_scalar(log_rel[:], log_rel[:], 0.0, None, ALU.max).then_inc(cut_made, 1)
            dve.wait_ge(threshold_made, 1)
            nc.vector.tensor_scalar(denominator[:], denominator[:], threshold[:, 0:1], None, ALU.max).then_inc(cut_made, 1)
            dve.wait_ge(log_made, 2)
            nc.vector.tensor_scalar(denominator[:], denominator[:], EPS, None, ALU.add).then_inc(setup_step, 1)
            dve.wait_ge(setup_step, 2)
            nc.vector.reciprocal(row_scale[:], denominator[:]).then_inc(setup_step, 1)
            dve.wait_ge(setup_step, 3)
            nc.vector.tensor_scalar(row_scale[:], row_scale[:], W1_col[:, 0:1], None, ALU.mult).then_inc(scale_made, 1)
            dve.wait_ge(product_far_ready, 1)
            nc.vector.tensor_tensor(bias_far[:], psum[:, 0, 0:1], b2_col[:], ALU.add).then_inc(bias_far_ready, 1)
            dve.wait_ge(bias_far_ready, 1)

            def add_bias(n, turn):
                dve.wait_ge(x_loaded[n], (turn + 1) * 16)
                if WIDTH[n] < S:
                    far = x_tile[:, n, WIDTH[n]:S]
                    nc.vector.tensor_scalar(far, far, bias_far[:, 0:1], None, ALU.add).then_inc(far_added[n], 1)
                near = x_tile[:, n, 0:WIDTH[n]]
                dve.wait_ge(product_ready[n], turn + 1)
                nc.vector.scalar_tensor_tensor(near, psum[:, n % 2, 0:WIDTH[n]], b2_col[:, 0:1], near,
                                               ALU.add, ALU.add).then_inc(near_added[n], 1)

            with dve.Fori(0, TURNS) as turn:
                for n in range(BANDS):
                    add_bias(n, turn)

        @block.scalar
        def _(act):
            act.wait_ge(params_loaded, 6 * 16)
            nc.scalar.activation(threshold[:], init_col[:], ACT.Abs, scale=multiplier_col[:, 0:1]).then_inc(threshold_made, 1)
            nc.scalar.activation(hidden_far[:], b1_col[:, 0:1].to_broadcast([P, 2]), ACT.Relu).then_inc(hidden_far_ready, 1)
            act.wait_ge(cut_made, 1)
            nc.scalar.activation(log_rel[:], log_rel[:], ACT.Abs, scale=c_col[:, 0:1]).then_inc(abs_made, 1)
            act.wait_ge(abs_made, 1)
            nc.scalar.activation(log_rel[:], log_rel[:], ACT.Ln, bias=1.0).then_inc(log_made, 1)
            act.wait_ge(cut_made, 2)
            nc.scalar.activation(denominator[:], denominator[:], ACT.Abs, scale=c_col[:, 0:1]).then_inc(abs_made, 1)
            act.wait_ge(abs_made, 2)
            nc.scalar.activation(denominator[:], denominator[:], ACT.Ln, bias=1.0).then_inc(log_made, 1)
            act.wait_ge(log_made, 2)
            act.wait_ge(scale_made, 1)

            def relu_tile(n, turn):
                wait_two_back(act, product_ready, n, turn)
                scales = row_scale[:, :].rearrange("p (b t g) -> p b t g", b=BANDS, g=GROUPS)
                for g in range(GROUPS):
                    first = SHIFT - ORDER[n] * BAND_ROWS - (TURNS - 1) * TILE_ROWS - g * GROUP_ROWS
                    logs = log_rel[:, first:first + (TURNS - 1) * TILE_ROWS + WIDTH[n]]
                    nc.scalar.activation(
                        hidden[:, n % 2, g, 0:WIDTH[n]], logs[:, bass.ds((TURNS - 1 - turn) * TILE_ROWS, WIDTH[n])], ACT.Relu,
                        bias=b1_col[:, 0:1], scale=scales[:, ORDER[n], bass.ds(turn, 1), g]).then_inc(hidden_ready[n], 1)

            for n in range(BANDS):
                relu_tile(n, 0)
            with act.Fori(1, TURNS) as turn:
                for n in range(BANDS):
                    relu_tile(n, turn)

        @block.tensor
        def _(pe):
            pe.wait_ge(W2_ready, GROUPS * GROUP_ROWS)
            pe.wait_ge(hidden_far_ready, 1)
            for g in range(GROUPS):
                product = nc.tensor.matmul(psum[:, 0, 0:2], W2_spread[:, g, :, :].rearrange("p h r -> p (h r)"),
                                           hidden_far[:], start=(g == 0), stop=(g == GROUPS - 1))
            product.then_inc(product_far_ready, 1)
            pe.wait_ge(bias_far_ready, 1)

            def multiply(n, turn):
                pe.wait_ge(hidden_ready[n], (turn + 1) * GROUPS)
                wait_two_back(pe, near_added, n, turn)
                for k in range(0, WIDTH[n], BANK):
                    end = min(k + BANK, WIDTH[n])
                    for g in range(GROUPS):
                        product = nc.tensor.matmul(psum[:, n % 2, k:end], W2_spread[:, g, :, :].rearrange("p h r -> p (h r)"),
                                                   hidden[:, n % 2, g, k:end], start=(g == 0), stop=(g == GROUPS - 1))
                product.then_inc(product_ready[n], 1)

            for n in range(BANDS):
                multiply(n, 0)
            with pe.Fori(1, TURNS) as turn:
                for n in range(BANDS):
                    multiply(n, turn)


_INS = ["x", "L0_conv_W1", "L0_conv_b1", "L0_conv_W2", "L0_conv_b2", "L0_conv_c", "L0_conv_L_multiplier",
        "L0_conv_init_L"]


def kernel(**inputs):
    import numpy as _np
    import concourse.bacc as _bacc
    from concourse import mybir as _mybir
    from concourse.bass_utils import run_bass_kernel_spmd as _run

    nc = _bacc.Bacc("TRN2", target_bir_lowering=False, num_devices=1)
    arrays, args = {}, []
    for name in _INS:
        a = _np.ascontiguousarray(inputs[name])
        a = a.reshape(a.shape or (1,))
        arrays[f"in_{name}_dram"] = a
        args.append(nc.dram_tensor(f"in_{name}_dram", a.shape, _mybir.dt.from_np(a.dtype), kind="ExternalInput").ap())
    out_shape = arrays["in_x_dram"].shape
    args.append(nc.dram_tensor("out_0_dram", out_shape, _mybir.dt.float32, kind="ExternalOutput").ap())
    fire_bias_kernel(nc, *args)
    r = _run(nc, [arrays], core_ids=[0])
    return r.results[0]["out_0_dram"]
```

```python
from contextlib import ExitStack

import concourse.bass as bass
from concourse import mybir

ALU = mybir.AluOpType
ACT = mybir.ActivationFunctionType
F32 = mybir.dt.float32
P = 128
QUADRANT = 32
BANK = 512


def fire_bias_kernel(nc, x, unit_params, b2, scalars, out):
    EPS = 1e-6
    _, H, S, _ = x.shape
    M = unit_params.shape[0]
    GROUP_ROWS = P // M
    GROUPS = P // QUADRANT
    TILE_ROWS = GROUPS * GROUP_ROWS
    TILE_HEADS = P // TILE_ROWS
    HEAD_SETS = H // TILE_HEADS
    BANDS = 8
    BAND_ROWS = S // BANDS
    TURNS = BAND_ROWS // TILE_ROWS
    TILES = BANDS * HEAD_SETS
    BUFFERS = 8
    USES = TILES // BUFFERS
    AHEAD = BUFFERS // 2
    assert M == QUADRANT and GROUP_ROWS * TILE_HEADS == QUADRANT and HEAD_SETS == 2
    ORDER = [band for n in range(BANDS // 2) for band in (n, BANDS - 1 - n)]
    WIDTH = [(band + 1) * BAND_ROWS for band in ORDER]

    SHIFT = S - GROUP_ROWS
    TABLE = SHIFT + BAND_ROWS

    with ExitStack() as ctx:
        def sb(name, shape):
            return ctx.enter_context(nc.sbuf_tensor(name, shape, F32))

        def sem(name):
            return ctx.enter_context(nc.semaphore(name))

        x_tile = sb("x_tile", [P, BUFFERS, S])
        hidden = sb("hidden", [P, 2, GROUPS, S])
        log_rel = sb("log_rel", [P, TABLE])
        row_scale = sb("row_scale", [P, S // GROUP_ROWS])
        denominator = sb("denominator", [P, S // GROUP_ROWS])
        row_in_group = sb("row_in_group", [P, 1])
        threshold = sb("threshold", [P, 1])
        abs_c = sb("abs_c", [P, 1])
        scalar_cols = sb("scalar_cols", [P, 3])
        c_col, multiplier_col, init_col = (scalar_cols[:, i:i + 1] for i in range(3))
        unit_rows = sb("unit_rows", [P, H + 2])
        W2_rows, W1_col, b1_col = unit_rows[:, 0:H], unit_rows[:, H:H + 1], unit_rows[:, H + 1:H + 2]
        b2_col = sb("b2_col", [P, HEAD_SETS])
        W2_spread = sb("W2_spread", [P, HEAD_SETS, GROUP_ROWS, TILE_HEADS])
        hidden_far = sb("hidden_far", [P, 2])
        bias_far = sb("bias_far", [P, HEAD_SETS])
        psum = ctx.enter_context(nc.psum_tensor("bias", [P, HEAD_SETS, S], F32))

        scalars_loaded = sem("scalars_loaded")
        units_loaded = sem("units_loaded")
        b2_loaded = sem("b2_loaded")
        iota_made = sem("iota_made")
        row_made = sem("row_made")
        abs_made = sem("abs_made")
        rel_made = sem("rel_made")
        pos_made = sem("pos_made")
        log_made = sem("log_made")
        denominator_made = sem("denominator_made")
        scale_made = sem("scale_made")
        zeros_made = sem("zeros_made")
        W2_ready = sem("W2_ready")
        hidden_far_ready = sem("hidden_far_ready")
        product_far_ready = sem("product_far_ready")
        bias_far_ready = sem("bias_far_ready")
        x_loaded = [sem(f"x_loaded{n}") for n in range(BUFFERS)]
        x_stored = [sem(f"x_stored{n}") for n in range(BUFFERS)]
        hidden_ready = [sem(f"hidden_ready{n}") for n in range(BANDS)]
        product_ready = [sem(f"product_ready{n}") for n in range(TILES)]
        near_added = [sem(f"near_added{n}") for n in range(TILES)]
        far_added = [sem(f"far_added{n}") for n in range(TILES)]

        def tile_of(tensor, n, turn):
            band, heads = ORDER[n // HEAD_SETS], n % HEAD_SETS
            rows = tensor[0, heads * TILE_HEADS:(heads + 1) * TILE_HEADS, band * BAND_ROWS:(band + 1) * BAND_ROWS, :]
            return rows[:, bass.ds(turn * TILE_ROWS, TILE_ROWS), :].rearrange("h r k -> r h k")

        def use(n, turn):
            return turn * USES + n // BUFFERS

        def wait_earlier(engine, done, n, back, turn):
            if n >= back:
                engine.wait_ge(done[n - back], turn + 1)
            elif not isinstance(turn, int):
                engine.wait_ge(done[n - back + TILES], turn)

        block = ctx.enter_context(nc.Block())

        @block.sync
        def _(sp):
            def load(n, turn):
                sp.dma_start(x_tile[:, n % BUFFERS, :], tile_of(x, n, turn)).then_inc(x_loaded[n % BUFFERS], 16)

            def reload(n, turn):
                sp.wait_ge(x_stored[n % BUFFERS], use(n, turn) * 16)
                load(n, turn)

            def store(n, turn):
                sp.wait_ge(near_added[n], turn + 1)
                if WIDTH[n // HEAD_SETS] < S:
                    sp.wait_ge(far_added[n], turn + 1)
                sp.dma_start(tile_of(out, n, turn), x_tile[:, n % BUFFERS, :]).then_inc(x_stored[n % BUFFERS], 16)

            sp.dma_start(scalar_cols[:], scalars.partition_broadcast(P)).then_inc(scalars_loaded, 16)
            sp.dma_start(unit_rows[:], bass.AP(unit_params.tensor, 0, [[0, GROUP_ROWS], [H + 2, M], [1, H + 2]])).then_inc(units_loaded, 16)
            sp.dma_start(b2_col[:], bass.AP(b2.tensor, 0, [[0, TILE_ROWS], [HEAD_SETS, TILE_HEADS], [1, HEAD_SETS]])).then_inc(b2_loaded, 16)
            for n in range(BUFFERS):
                load(n, 0)
            for n in range(TILES):
                store(n, 0)
                if n + AHEAD >= TILES:
                    reload(n + AHEAD - TILES, 1)
                elif n + AHEAD >= BUFFERS:
                    reload(n + AHEAD, 0)
            with sp.Fori(1, TURNS - 1) as turn:
                for n in range(TILES):
                    store(n, turn)
                    if n + AHEAD < TILES:
                        reload(n + AHEAD, turn)
                    else:
                        reload(n + AHEAD - TILES, turn + 1)
            for n in range(TILES):
                store(n, TURNS - 1)
                if n + AHEAD < TILES:
                    reload(n + AHEAD, TURNS - 1)
            for n in range(BUFFERS):
                sp.wait_ge(x_stored[n], TURNS * USES * 16)

        @block.gpsimd
        def _(pool):
            nc.gpsimd.iota(log_rel[:], [[-1, TABLE]], base=SHIFT, channel_multiplier=0,
                           allow_small_or_imprecise_dtypes=True).then_inc(iota_made, 1)
            nc.gpsimd.iota(denominator[:], [[GROUP_ROWS, S // GROUP_ROWS]], base=0, channel_multiplier=0,
                           allow_small_or_imprecise_dtypes=True).then_inc(iota_made, 1)

        @block.vector
        def _(dve):
            for r in range(GROUP_ROWS):
                nc.vector.memset(row_in_group[r * M:(r + 1) * M, :], float(r)).then_inc(row_made, 1)
            nc.vector.memset(W2_spread[:], 0.0).then_inc(zeros_made, 1)
            dve.wait_ge(row_made, GROUP_ROWS)
            dve.wait_ge(iota_made, 1)
            nc.vector.tensor_scalar(log_rel[:], log_rel[:], row_in_group[:, 0:1], 0.0, ALU.add, ALU.max).then_inc(rel_made, 1)
            dve.wait_ge(iota_made, 2)
            dve.wait_ge(abs_made, 2)
            nc.vector.tensor_scalar(denominator[:], denominator[:], row_in_group[:, 0:1], threshold[:, 0:1],
                                    ALU.add, ALU.max).then_inc(pos_made, 1)
            dve.wait_ge(zeros_made, 1)
            dve.wait_ge(units_loaded, 16)
            for r in range(GROUP_ROWS):
                rows = slice(r * M, (r + 1) * M)
                nc.vector.tensor_copy(W2_spread[rows, :, r, :],
                                      W2_rows[rows, :].rearrange("m (s h) -> m s h", s=HEAD_SETS)).then_inc(W2_ready, 1)
            dve.wait_ge(log_made, 1)
            nc.vector.tensor_scalar(denominator[:], denominator[:], EPS, None, ALU.add).then_inc(denominator_made, 1)
            dve.wait_ge(denominator_made, 1)
            nc.vector.reciprocal(denominator[:], denominator[:]).then_inc(denominator_made, 1)
            dve.wait_ge(denominator_made, 2)
            nc.vector.tensor_scalar(row_scale[:], denominator[:], W1_col, None, ALU.mult).then_inc(scale_made, 1)
            dve.wait_ge(b2_loaded, 16)
            dve.wait_ge(product_far_ready, 1)
            nc.vector.tensor_tensor(bias_far[:], psum[:, :, 0], b2_col[:], ALU.add).then_inc(bias_far_ready, 1)
            dve.wait_ge(bias_far_ready, 1)

            def add_bias(n, turn):
                heads, width = n % HEAD_SETS, WIDTH[n // HEAD_SETS]
                dve.wait_ge(x_loaded[n % BUFFERS], (use(n, turn) + 1) * 16)
                if width < S:
                    far = x_tile[:, n % BUFFERS, width:S]
                    nc.vector.tensor_scalar(far, far, bias_far[:, heads:heads + 1], None, ALU.add).then_inc(far_added[n], 1)
                near = x_tile[:, n % BUFFERS, 0:width]
                dve.wait_ge(product_ready[n], turn + 1)
                nc.vector.scalar_tensor_tensor(near, psum[:, heads, 0:width], b2_col[:, heads:heads + 1], near,
                                               ALU.add, ALU.add).then_inc(near_added[n], 1)

            with dve.Fori(0, TURNS) as turn:
                for n in range(TILES):
                    add_bias(n, turn)

        @block.scalar
        def _(act):
            act.wait_ge(scalars_loaded, 16)
            nc.scalar.activation(abs_c[:], c_col, ACT.Abs).then_inc(abs_made, 1)
            nc.scalar.activation(threshold[:], init_col, ACT.Abs, scale=multiplier_col).then_inc(abs_made, 1)
            act.wait_ge(abs_made, 1)
            act.wait_ge(pos_made, 1)
            nc.scalar.activation(denominator[:], denominator[:], ACT.Ln, bias=1.0, scale=abs_c[:, 0:1]).then_inc(log_made, 1)
            act.wait_ge(rel_made, 1)
            nc.scalar.activation(log_rel[:], log_rel[:], ACT.Ln, bias=1.0, scale=abs_c[:, 0:1]).then_inc(log_made, 1)
            act.wait_ge(units_loaded, 16)
            nc.scalar.activation(hidden_far[:], b1_col.to_broadcast([P, 2]), ACT.Relu).then_inc(hidden_far_ready, 1)
            act.wait_ge(log_made, 2)
            act.wait_ge(scale_made, 1)

            scales = row_scale[:, :].rearrange("p (b t g) -> p b t g", b=BANDS, g=GROUPS)

            def relu_rows(m, turn):
                band, width = ORDER[m], WIDTH[m]
                wait_earlier(act, product_ready, m * HEAD_SETS + HEAD_SETS - 1, 2 * HEAD_SETS, turn)
                for g in range(GROUPS):
                    first = SHIFT - band * BAND_ROWS - (TURNS - 1) * TILE_ROWS - g * GROUP_ROWS
                    logs = log_rel[:, first:first + (TURNS - 1) * TILE_ROWS + width]
                    nc.scalar.activation(
                        hidden[:, m % 2, g, 0:width], logs[:, bass.ds((TURNS - 1 - turn) * TILE_ROWS, width)], ACT.Relu,
                        bias=b1_col, scale=scales[:, band, bass.ds(turn, 1), g]).then_inc(hidden_ready[m], 1)

            for m in range(BANDS):
                relu_rows(m, 0)
            with act.Fori(1, TURNS) as turn:
                for m in range(BANDS):
                    relu_rows(m, turn)

        @block.tensor
        def _(pe):
            def products(heads, moving, columns):
                for g in range(GROUPS):
                    last = nc.tensor.matmul(psum[g * QUADRANT:(g + 1) * QUADRANT, heads, columns],
                                            W2_spread[:, heads, :, :].rearrange("p r h -> p (r h)"), moving(g),
                                            start=True, stop=True)
                return last

            pe.wait_ge(W2_ready, GROUP_ROWS)
            pe.wait_ge(hidden_far_ready, 1)
            for heads in range(HEAD_SETS):
                last = products(heads, lambda g: hidden_far[:], slice(0, 2))
            last.then_inc(product_far_ready, 1)
            pe.wait_ge(bias_far_ready, 1)

            def multiply(n, turn):
                m, heads = n // HEAD_SETS, n % HEAD_SETS
                if heads == 0:
                    pe.wait_ge(hidden_ready[m], (turn + 1) * GROUPS)
                wait_earlier(pe, near_added, n, HEAD_SETS, turn)
                for k in range(0, WIDTH[m], BANK):
                    columns = slice(k, min(k + BANK, WIDTH[m]))
                    last = products(heads, lambda g: hidden[:, m % 2, g, columns], columns)
                last.then_inc(product_ready[n], 1)

            for n in range(TILES):
                multiply(n, 0)
            with pe.Fori(1, TURNS) as turn:
                for n in range(TILES):
                    multiply(n, turn)


def kernel(**inputs):
    import numpy as np
    import concourse.bacc as bacc
    from concourse.bass_utils import run_bass_kernel_spmd

    x, W1, b1, W2, b2, c, L_multiplier, init_L = (np.asarray(inputs[name]) for name in (
        "x", "L0_conv_W1", "L0_conv_b1", "L0_conv_W2", "L0_conv_b2", "L0_conv_c", "L0_conv_L_multiplier",
        "L0_conv_init_L"))
    arrays = {
        "x": np.ascontiguousarray(x),
        "unit_params": np.concatenate([W2, W1.reshape(-1, 1), b1.reshape(-1, 1)], axis=1),
        "b2": np.ascontiguousarray(b2.reshape(2, -1).T),
        "scalars": np.stack([c, L_multiplier, init_L]),
    }
    nc = bacc.Bacc("TRN2", target_bir_lowering=False, num_devices=1)
    args = [nc.dram_tensor(name, a.shape, mybir.dt.from_np(a.dtype), kind="ExternalInput").ap()
            for name, a in arrays.items()]
    out = nc.dram_tensor("out", x.shape, F32, kind="ExternalOutput").ap()
    fire_bias_kernel(nc, *args, out)
    r = run_bass_kernel_spmd(nc, [arrays], core_ids=[0])
    return r.results[0]["out"]
```
